# Optimizing a Trainium2 kernel written in Bass

```python
import numpy as np
import jax
import jax.numpy as jnp

def _softmax(x, axis=-1):
    return jax.nn.softmax(x, axis=axis)

def _gelu(x):
    return jax.nn.gelu(x, approximate=True)

def _silu(x):
    return jax.nn.silu(x)

def _sigmoid(x):
    return jax.nn.sigmoid(x)

def _layernorm(x, axis=-1, eps=1e-05):
    m = jnp.mean(x, axis=axis, keepdims=True)
    v = jnp.var(x, axis=axis, keepdims=True)
    return (x - m) / jnp.sqrt(v + eps)

def _scatter_add(tgt, idx, src, axis=0):
    return tgt.at[idx].add(src)

def _segment_sum(src, seg, n):
    return jax.ops.segment_sum(src, seg, n)
kernel_name = 'mk_recurrent_d1_jaxref_r4_cfdb0b'

def setup_inputs(seed: int=0):
    np.random.seed(seed)
    _w = jnp.asarray

    def _L0_attn_setup():
        import jax, jax.numpy as jnp
        import numpy as np
        B, T, D, H = (4, 512, 256, 16)
        HD = D // H

        def l2_norm(x, eps=1e-12):
            return x / jnp.maximum(jnp.linalg.norm(x, axis=-1, keepdims=True), eps)
        key = jax.random.key(seed)
        ks = jax.random.split(key, 11)
        std = 0.02
        w = lambda k, shape: jax.random.normal(k, shape, jnp.float32) * std
        return dict(x=jax.random.normal(ks[0], (B, T, D), jnp.float32), Wq=w(ks[1], (D, D)), Wk=w(ks[2], (D, D)), Wv=w(ks[3], (D, D)), Wgamma=w(ks[4], (D, H)), Wf1=w(ks[5], (D, HD)), Wf2=w(ks[6], (HD, D)), Wog1=w(ks[7], (D, HD)), Wog2=w(ks[8], (HD, D)), norm_w=jnp.ones((D,), jnp.float32), Wo=w(ks[9], (D, D)))
    _L0_attn_in = _L0_attn_setup()

    def _L0_ffn_setup():
        import jax, jax.numpy as jnp
        import numpy as np
        B, S, D = (2, 512, 256)
        E, K, DFF = (8, 2, 4 * 256)
        EPS_GATE = 1e-08
        EPS_LN = 1e-05
        key = jax.random.key(seed)
        ks = jax.random.split(key, 4)
        scaled = lambda k, shape, fan: jax.random.normal(k, shape, jnp.float32) / np.sqrt(fan).astype(np.float32)
        return {'x': jax.random.normal(ks[0], (B, S, D), jnp.float32), 'Wg': scaled(ks[1], (D, E), D), 'bg': jnp.zeros((E,), jnp.float32), 'W1': scaled(ks[2], (E, D, DFF), D), 'b1': jnp.zeros((E, DFF), jnp.float32), 'W2': scaled(ks[3], (E, DFF, D), DFF), 'b2': jnp.zeros((E, D), jnp.float32), 'gamma': jnp.ones((D,), jnp.float32), 'beta': jnp.zeros((D,), jnp.float32)}
    _L0_ffn_in = _L0_ffn_setup()
    _d = {'L0_attn_x': _L0_attn_in['x'], 'L0_attn_Wq': _L0_attn_in['Wq'], 'L0_attn_Wk': _L0_attn_in['Wk'], 'L0_attn_Wv': _L0_attn_in['Wv'], 'L0_attn_Wgamma': _L0_attn_in['Wgamma'], 'L0_attn_Wf1': _L0_attn_in['Wf1'], 'L0_attn_Wf2': _L0_attn_in['Wf2'], 'L0_attn_Wog1': _L0_attn_in['Wog1'], 'L0_attn_Wog2': _L0_attn_in['Wog2'], 'L0_attn_norm_w': _L0_attn_in['norm_w'], 'L0_attn_Wo': _L0_attn_in['Wo'], 'L0_ffn_Wg': _L0_ffn_in['Wg'], 'L0_ffn_bg': _L0_ffn_in['bg'], 'L0_ffn_W1': _L0_ffn_in['W1'], 'L0_ffn_b1': _L0_ffn_in['b1'], 'L0_ffn_W2': _L0_ffn_in['W2'], 'L0_ffn_b2': _L0_ffn_in['b2'], 'L0_ffn_gamma': _L0_ffn_in['gamma'], 'L0_ffn_beta': _L0_ffn_in['beta']}
    _x0 = _d['L0_attn_x']
    _d['L0_attn_x'] = jax.random.normal(jax.random.fold_in(jax.random.key(seed), 1), (8, 512, 256), dtype=_x0.dtype)
    del _x0
    return _d

def reference(L0_attn_x, L0_attn_Wq, L0_attn_Wk, L0_attn_Wv, L0_attn_Wgamma, L0_attn_Wf1, L0_attn_Wf2, L0_attn_Wog1, L0_attn_Wog2, L0_attn_norm_w, L0_attn_Wo, L0_ffn_Wg, L0_ffn_bg, L0_ffn_W1, L0_ffn_b1, L0_ffn_W2, L0_ffn_b2, L0_ffn_gamma, L0_ffn_beta):

    def _L0_attn_ref(x, Wq, Wk, Wv, Wgamma, Wf1, Wf2, Wog1, Wog2, norm_w, Wo):
        import jax, jax.numpy as jnp
        import numpy as np
        B, T, D, H = (4, 512, 256, 16)
        HD = D // H

        def l2_norm(x, eps=1e-12):
            return x / jnp.maximum(jnp.linalg.norm(x, axis=-1, keepdims=True), eps)
        b, n, d = x.shape
        q = jax.nn.silu(x @ Wq)
        k = jax.nn.silu(x @ Wk)
        v = x @ Wv
        log_f = jax.nn.log_sigmoid(x @ Wf1 @ Wf2)
        gamma = -jax.nn.sigmoid(x @ Wgamma)
        q = q.reshape(b, n, H, HD)
        k = l2_norm(k.reshape(b, n, H, HD))
        v = v.reshape(b, n, H, HD)
        gk = log_f.reshape(b, n, H, HD)
        a = k * gamma[..., None] * jnp.exp(gk)

        def step(S, inp):
            qt, kt, vt, at, gkt = inp
            S = S * jnp.exp(gkt)[..., None]
            sab = jnp.einsum('bhk,bhkv->bhv', at, S)
            S = S + kt[..., None] * (sab[..., None, :] + vt[..., None, :])
            ot = jnp.einsum('bhk,bhkv->bhv', qt, S)
            return (S, ot)
        seq = tuple((jnp.moveaxis(t, 1, 0) for t in (q, k, v, a, gk)))
        S0 = jnp.zeros((b, H, HD, HD), x.dtype)
        _, o = jax.lax.scan(step, S0, seq)
        o = jnp.moveaxis(o, 0, 1).reshape(b, n, d)
        o = o * jax.nn.sigmoid(x @ Wog1 @ Wog2)
        mu = o.mean(-1, keepdims=True)
        var = ((o - mu) ** 2).mean(-1, keepdims=True)
        o = (o - mu) * jax.lax.rsqrt(var + 1e-05) * norm_w
        return o @ Wo

    def _L0_ffn_ref(x, Wg, bg, W1, b1, W2, b2, gamma, beta):
        import jax, jax.numpy as jnp
        import numpy as np
        B, S, D = (2, 512, 256)
        E, K, DFF = (8, 2, 4 * 256)
        EPS_GATE = 1e-08
        EPS_LN = 1e-05
        b, s, d = x.shape
        xf = x.reshape(-1, d)
        T = xf.shape[0]
        num_experts = Wg.shape[1]
        logits = xf @ Wg + bg
        w = jax.nn.softmax(logits, axis=-1)
        top_w, top_idx = jax.lax.top_k(w, K)
        top_w = top_w / (top_w.sum(axis=-1, keepdims=True) + EPS_GATE)
        cw = jnp.zeros((T, num_experts), xf.dtype).at[jnp.arange(T)[:, None], top_idx].add(top_w)
        out = jnp.zeros_like(xf)
        for e in range(num_experts):
            h = jax.nn.gelu(xf @ W1[e] + b1[e], approximate=False)
            y = h @ W2[e] + b2[e]
            out = out + cw[:, e:e + 1] * y
        mu = out.mean(axis=-1, keepdims=True)
        var = out.var(axis=-1, keepdims=True)
        out = (out - mu) / jnp.sqrt(var + EPS_LN) * gamma + beta
        return out.reshape(b, s, d)
    x = L0_attn_x
    xn = _layernorm(x, axis=-1)
    s = _L0_attn_ref(xn, L0_attn_Wq, L0_attn_Wk, L0_attn_Wv, L0_attn_Wgamma, L0_attn_Wf1, L0_attn_Wf2, L0_attn_Wog1, L0_attn_Wog2, L0_attn_norm_w, L0_attn_Wo)
    g = _silu(_L0_ffn_ref(xn, L0_ffn_Wg, L0_ffn_bg, L0_ffn_W1, L0_ffn_b1, L0_ffn_W2, L0_ffn_b2, L0_ffn_gamma, L0_ffn_beta))
    x = x + s * g
    return x

_drawn_inputs = setup_inputs


def setup_inputs(seed=0):
    import zlib

    import numpy as np

    out = dict(_drawn_inputs(seed))
    spreads = {'L0_attn_norm_w': (1.0, 0.2),
     'L0_ffn_bg': (0.0, 0.1),
     'L0_ffn_b1': (0.0, 0.365),
     'L0_ffn_b2': (0.0, 0.1),
     'L0_ffn_gamma': (1.0, 0.2),
     'L0_ffn_beta': (0.0, 0.404)}
    factors = {'L0_attn_Wgamma': 8.0,
     'L0_attn_Wf1': 8.0,
     'L0_attn_Wf2': 8.0,
     'L0_attn_Wog1': 8.0,
     'L0_attn_Wog2': 8.0}
    for name, (base, spread) in spreads.items():
        noise = np.random.default_rng([zlib.crc32(name.encode()), seed]).standard_normal(out[name].shape)
        drawn = base * np.exp(spread * noise) if base else spread * noise
        out[name] = jnp.asarray(drawn.astype(out[name].dtype))
    for name, factor in factors.items():
        out[name] = (out[name] * factor).astype(out[name].dtype)
    return out
```

```python
from contextlib import ExitStack

import concourse.bass as bass
from concourse import mybir

F32 = mybir.dt.float32
ALU = mybir.AluOpType
ACT = mybir.ActivationFunctionType
AX = mybir.AxisListType

P = 128
B, T, D = 8, 512, 256
H, HD = 16, 16
E, DFF = 8, 1024
KC = D // P
FC = DFF // P
NT = B * T // P
NTB = T // P
REC = 5 * HD
A_, F_, K_, Q_, V_ = (HD * n for n in range(5))
MT = 256
MH = MT // P
NM = (2 * B * T - E) // MT + E
VH = HD // 2
RING = 16
HALF = RING // 2
NCH = T // RING
S_OFF = HD * HD + HD
SLOT = 2 * S_OFF
EPS = 1e-5
ZR = 3
ZP = NM * MT // NT // ZR
RS = 4
SL = 4


def build(nc, x, wq, wk, wv, wgamma, wf1, wf2, wog1, wog2, norm_w, wo,
          wg, bg, w1, b1, w2, b2, gamma, beta, out):
    ctx = ExitStack()
    with ctx:
        def sb(name, shape):
            return ctx.enter_context(nc.sbuf_tensor(name, shape, F32))

        def ps(name, shape):
            return ctx.enter_context(nc.psum_tensor(name, shape, F32))

        def sem(name):
            return ctx.enter_context(nc.semaphore(name))

        rec_d = nc.dram_tensor("rec_d", [B, T, H, REC], F32, kind="Internal").ap()
        xs_d = nc.dram_tensor("xs_d", [NM * MT, D], F32, kind="Internal").ap()
        y_d = nc.dram_tensor("y_d", [NM * MT, D], F32, kind="Internal").ap()
        og_d = nc.dram_tensor("og_d", [NT, P, D], F32, kind="Internal").ap()
        o_d = nc.dram_tensor("o_d", [B, T, D], F32, kind="Internal").ap()

        x_acc = sb("x_acc", [P, NT, D])
        ident = sb("ident", [P, P])
        tri = sb("tri", [P, P])
        ones = sb("ones", [P, P])
        zero = sb("zero", [ZP, ZR * D])
        w_kq = sb("w_kq", [P, KC, 2 * D])
        w_vgg = sb("w_vgg", [P, KC, D + H + E])
        w_low = sb("w_low", [P, KC, 2 * HD])
        w_up = sb("w_up", [2 * HD, 2 * D])
        wo_sb = sb("wo_sb", [P, KC, D])
        nw = sb("nw", [P, KC])
        wts = sb("wts", [P, 2 * 2 * KC * DFF])
        w1_sb = [wts[:, 2 * n * KC * DFF:(2 * n + 1) * KC * DFF].rearrange("p (c n) -> p c n", c=KC) for n in range(2)]
        w2_sb = [wts[:, (2 * n + 1) * KC * DFF:(2 * n + 2) * KC * DFF].rearrange("p (m n) -> p m n", m=FC)
                 for n in range(2)]
        b1_rows = sb("b1_rows", [E * FC, P])
        b1_sb = sb("b1_sb", [P, E * FC])
        b2_sb = sb("b2_sb", [1, E, D])
        bg_bc = sb("bg_bc", [P, E])
        gam_bc = sb("gam_bc", [P, D])
        bet_bc = sb("bet_bc", [P, D])
        stats = sb("stats", [P, NT, 6])
        mean = sb("mean", [P, NT])
        var = sb("var", [P, NT])
        rstd = sb("rstd", [P, NT])
        lt = sb("lt", [P, 4, B])
        neghalf = sb("neghalf", [P, NT])
        inv_d = sb("inv_d", [P, 2])
        logits = sb("logits", [P, NT, E])
        gw = sb("gw", [P, 5, NT, E])
        gs = sb("gs", [P, 6, NT])
        down8 = sb("down8", [P, E])
        xn = sb("xn", [P, 2, D])
        xTs = [sb(f"xTs{n}", [P, KC, P]) for n in range(2)]
        t1 = [sb(f"t1_{n}", [2 * HD, P]) for n in range(2)]
        work = sb("work", [P, 32 * D])
        rec = work[:, 0:RS * H * REC].rearrange("p (u h c) -> p u h c", u=RS, h=H)
        o1 = RS * H * REC
        sg = work[:, o1:o1 + 4 * D].rearrange("p (u n) -> p u n", u=2)
        kraw = work[:, o1 + 4 * D:o1 + 6 * D].rearrange("p (u n) -> p u n", u=2)
        f2 = work[:, o1 + 6 * D:o1 + 8 * D].rearrange("p (u n) -> p u n", u=2)
        ogs = work[:, o1 + 8 * D:o1 + 10 * D].rearrange("p (u n) -> p u n", u=2)
        ksq = work[:, o1 + 10 * D:o1 + 11 * D]
        kgam = work[:, o1 + 11 * D:o1 + 12 * D]
        ss = sb("ss", [P, 2, H])
        ssm = sb("ssm", [P, 2, H])
        rinv = sb("rinv", [P, 2, H])
        gam = sb("gam", [P, 2, H])
        ngam = sb("ngam", [P, 2, H])
        hT = work[:, 0:FC * MT].rearrange("p (m t) -> p m t", m=FC)
        xg = [work[:, (FC + n * MH) * MT:(FC + (n + 1) * MH) * MT].rearrange("p (s d) -> p s d", s=MH) for n in range(2)]
        ysb = [work[:, (FC + (2 + n) * MH) * MT:(FC + (3 + n) * MH) * MT].rearrange("p (s d) -> p s d", s=MH)
               for n in range(2)]
        xgT = sb("xgT", [P, KC, MT])
        thr = sb("thr", [P, B * T // MT])
        tidx = sb("tidx", [P, NM])
        tot = sb("tot", [P, NT, E])
        cum = sb("cum", [P, NT, E])
        cmp16 = sb("cmp16", [P, E, B * T // MT])
        nte = sb("nte", [P, 3, E])
        cmpt = sb("cmpt", [P, NM, E - 1])
        etab_f = sb("etab_f", [P, NM])
        etab = ctx.enter_context(nc.sbuf_tensor("etab", [P, NM], mybir.dt.int32))
        slot = sb("slot", [P, NT, 2])
        idx = ctx.enter_context(nc.sbuf_tensor("idx", [P, 2 * NT], mybir.dt.uint32))
        wy = sb("wy", [P, 2, D])
        ym = sb("ym", [P, D])
        yn = sb("yn", [P, D])
        zg = sb("zg", [P, 2, D])
        szg = sb("szg", [P, 2, D])
        gst = sb("gst", [P, 5])
        ring = sb("ring", [P, RING, SLOT])
        rbh = sb("rbh", [P, 2, RING, REC])
        ubuf = sb("ubuf", [P, HD])
        qbuf = sb("qbuf", [P, HD * HD])
        obh = sb("obh", [P, 2, RING, HD])

        psA = [ps(f"psA{n}", [P, 512]) for n in range(2)]
        psB = [ps(f"psB{n}", [P, 512]) for n in range(2)]
        psF = [ps(f"psF{n}", [P, 512]) for n in range(2)]
        psT = [ps(f"psT{n}", [P, 512]) for n in range(2)]
        ph = [psA[0], psA[1], psB[0], psB[1]]


        cst = sb("cst", [P, SL, 6])
        cmv = sb("cmv", [P, SL, 3])
        cve = sb("cve", [P, SL])
        crs = sb("crs", [P, SL])
        oTs = xTs
        ring2 = ring[:, :, :].rearrange("p s (two c) -> p s two c", two=2)
        stats_flat = stats[:, :, :].rearrange("p t s -> p (t s)")
        sel = gw[:, 0, :, :].rearrange("p t e -> p (t e)")
        gs_flat = gs[:, :, :].rearrange("p v t -> p (v t)")
        b2_flat = b2_sb[:, :, :].rearrange("a e n -> a (e n)")
        ring_flat = ring[:, :, :].rearrange("p s c -> p (s c)")

        def slots(mem, n):
            return mem[:, n * SL * D:(n + 1) * SL * D].rearrange("p (u d) -> p u d", u=SL)

        fx, fo, fog, f_on, f_sg = (slots(work, n) for n in range(5))

        s_x = [sem(f"s_x{n}") for n in range(NTB)]
        s_w = sem("s_w")
        s_c = sem("s_c")
        s_pool0 = sem("s_pool0")
        s_id = sem("s_id")
        s_st = sem("s_st")
        s_stc = sem("s_stc")
        s_lt = sem("s_lt")
        s_var = sem("s_var")
        s_rstd = sem("s_rstd")
        s_xn = sem("s_xn")
        s_T = sem("s_T")
        s_xTs = sem("s_xTs")
        s_xTc = sem("s_xTc")
        s_L = sem("s_L")
        s_t1 = sem("s_t1")
        s_A = sem("s_A")
        s_Bp = sem("s_Bp")
        s_Fp = sem("s_Fp")
        s_sg = sem("s_sg")
        s_gam = sem("s_gam")
        s_v = sem("s_v")
        s_f = sem("s_f")
        s_og = sem("s_og")
        s_f2 = sem("s_f2")
        s_kq = sem("s_kq")
        s_ksq = sem("s_ksq")
        s_ssm = sem("s_ssm")
        s_lg = sem("s_lg")
        s_pA = sem("s_pA")
        s_ng = sem("s_ng")
        s_kg = sem("s_kg")
        s_rec = sem("s_rec")
        s_recd = [sem(f"s_recd{n}") for n in range(RS)]
        s_ogd = [sem(f"s_ogd{n}") for n in range(2)]
        s_gt = sem("s_gt")
        s_exp = sem("s_exp")
        s_dG = sem("s_dG")
        s_sel = sem("s_sel")
        s_cnt = sem("s_cnt")
        s_slot = sem("s_slot")
        s_zero = sem("s_zero")
        s_idx = sem("s_idx")
        s_sc = sem("s_sc")
        s_b1t = sem("s_b1t")
        s_b1 = sem("s_b1")
        s_w1d = [sem(f"s_w1d{n}") for n in range(2)]
        s_w2d = [sem(f"s_w2d{n}") for n in range(2)]
        s_xg = [sem(f"s_xg{n}") for n in range(2)]
        s_xgT = sem("s_xgT")
        s_xgs = sem("s_xgs")
        s_yd = [sem(f"s_yd{n}") for n in range(2)]
        s_gat = sem("s_gat")
        s_wy0 = sem("s_wy0")
        s_wy = sem("s_wy")
        s_ym = sem("s_ym")
        s_gA = sem("s_gA")
        s_sq = sem("s_sq")
        s_gP = sem("s_gP")
        s_yr = sem("s_yr")
        s_h = sem("s_h")
        s_hb = sem("s_hb")
        s_y = sem("s_y")
        s_ys = sem("s_ys")
        s_rb = [sem(f"s_rb{n}") for n in range(2)]
        s_vr = sem("s_vr")
        s_half = [sem(f"s_half{n}") for n in range(2)]
        s_om = sem("s_om")
        s_o = sem("s_o")
        s_od = [sem(f"s_od{n}") for n in range(2)]
        s_xl = [sem(f"s_xl{n}") for n in range(SL)]
        s_dC = sem("s_dC")
        s_v1 = sem("s_v1")
        s_r1 = sem("s_r1")
        s_on = sem("s_on")
        s_oT = sem("s_oT")
        s_oTs = sem("s_oTs")
        s_s = sem("s_s")
        s_yn = sem("s_yn")
        s_pC = sem("s_pC")
        s_z = sem("s_z")
        s_sz = sem("s_sz")
        s_g2 = sem("s_g2")
        s_sgm = sem("s_sgm")
        s_res = sem("s_res")
        s_out = [sem(f"s_out{n}") for n in range(SL)]

        x_v = x.rearrange("b (j p) d -> j b p d", p=P)
        out_v = out.rearrange("b (j p) d -> j b p d", p=P)
        rec_w = rec_d.rearrange("b (j p) h c -> j b p (h c)", p=P)
        rec_r = rec_d.rearrange("b t h c -> b h t c")
        o_w = o_d.rearrange("b t (h v) -> b h t v", v=HD)
        o_r = o_d.rearrange("b (j p) d -> j b p d", p=P)
        xs_z = xs_d.rearrange("(n p r) d -> n p (r d)", p=ZP, r=ZR)
        xs_v = xs_d.rearrange("(t s p) d -> t p s d", s=MH, p=P)
        y_v = y_d.rearrange("(t s p) d -> t p s d", s=MH, p=P)
        w1_v = w1.rearrange("e (c p) n -> e p c n", p=P)
        w2_v = w2.rearrange("e (m p) n -> e p m n", p=P)
        N_W, N_C = 10, 7

        block = ctx.enter_context(nc.Block())

        def per_tile(eng, step, s=2):
            for n in range(s):
                step(n, n, True, False)
            with eng.Fori(1, NT // s - 1) as turn:
                for u in range(s):
                    step(turn * s + u, u, False, False)
            for n in range(NT - s, NT):
                step(n, n % s, False, True)

        @block.sync
        def _(sp):
            for j in range(NTB):
                for b_ in range(B):
                    sp.dma_start(x_acc[:, j * B + b_, :], x_v[j, b_]).then_inc(s_x[j], 16)
                if j == 0:
                    for n, w in enumerate((wf1, wog1)):
                        sp.dma_start(w_low[:, :, n * HD:(n + 1) * HD], w.rearrange("(c p) n -> p c n", p=P)).then_inc(s_w, 16)
                    for n, w in enumerate((wk, wq)):
                        sp.dma_start(w_kq[:, :, n * D:(n + 1) * D], w.rearrange("(c p) n -> p c n", p=P)).then_inc(s_w, 16)
                    for w, lo, hi in ((wv, 0, D), (wgamma, D, D + H), (wg, D + H, D + H + E)):
                        sp.dma_start(w_vgg[:, :, lo:hi], w.rearrange("(c p) n -> p c n", p=P)).then_inc(s_w, 16)
                    sp.wait_ge(s_pool0, 1)
                    for n, w in enumerate((wf2, wog2)):
                        sp.dma_start(w_up[n * HD:(n + 1) * HD, n * D:(n + 1) * D], w).then_inc(s_w, 16)
                    sp.dma_start(bg_bc[:, :], bg.partition_broadcast(P)).then_inc(s_w, 16)
            sp.dma_start(wo_sb[:, :, :], wo.rearrange("(c p) n -> p c n", p=P)).then_inc(s_c, 16)
            for c in range(KC):
                sp.dma_start(nw[:, c:c + 1], norm_w.rearrange("(p a) -> p a", a=1)[c * P:(c + 1) * P]).then_inc(s_c, 16)
            sp.dma_start(b1_rows[:, :], b1.rearrange("e (m p) -> (e m) p", p=P)).then_inc(s_c, 16)
            sp.dma_start(b2_sb[:, :, :], b2.rearrange("(a e) n -> a e n", a=1)).then_inc(s_c, 16)
            sp.dma_start(gam_bc[:, :], gamma.partition_broadcast(P)).then_inc(s_c, 16)
            sp.dma_start(bet_bc[:, :], beta.partition_broadcast(P)).then_inc(s_c, 16)

            sp.wait_ge(s_pool0, 2)

            def spill(n, u4, first, last):
                u = u4 % 2
                sp.dma_start(xs_z[n], zero[:, :]).then_inc(s_zero, 16)
                sp.wait_ge(s_og, n + 1)
                sp.dma_start(og_d[n], ogs[:, u, :]).then_inc(s_ogd[u], 16)
                sp.wait_ge(s_rec, n + 1)
                sp.wait_ge(s_kq, n * 2 + 2)
                sp.wait_ge(s_f, n + 1)
                sp.wait_ge(s_v, n + 1)
                sp.dma_start(rec_w[n // B, n % B], rec[:, u4, :, :].rearrange("p h c -> p (h c)"))\
                    .then_inc(s_recd[u4], 16)

            per_tile(sp, spill, RS)
            for u in range(RS):
                sp.wait_ge(s_recd[u], 16 * (NT // RS))

            def load_chunk(c, u):
                for b_ in range(B):
                    sp.dma_start(rbh[b_ * H:(b_ + 1) * H, u, :, :], rec_r[b_, :, bass.ds(c * RING, RING), :])\
                        .then_inc(s_rb[u], 16)

            def store_chunk(c, u):
                for b_ in range(B):
                    sp.dma_start(o_w[b_, :, bass.ds(c * RING, RING), :], obh[b_ * H:(b_ + 1) * H, u, :, :])\
                        .then_inc(s_od[u], 16)

            for u in range(2):
                load_chunk(u, u)
            with sp.Fori(0, NCH // 2 - 1) as cp:
                for u in range(2):
                    sp.wait_ge(s_o, cp * 4 + 2 * u + 2)
                    load_chunk(cp * 2 + (u + 2), u)
                    store_chunk(cp * 2 + u, u)
            for c in range(NCH - 2, NCH):
                sp.wait_ge(s_o, 2 * c + 2)
                store_chunk(c, c % 2)
            for u in range(2):
                sp.wait_ge(s_yd[u], 16 * ((NM + 1 - u) // 2))
                sp.wait_ge(s_od[u], 16 * B * (NCH // 2))
                sp.wait_ge(s_ogd[u], 16 * (NT // 2))

            def store(n, u):
                sp.wait_ge(s_res, n + 1)
                sp.dma_start(out_v[n // B, n % B], fx[:, u, :]).then_inc(s_out[u], 16)

            def fetch(n, u, first, last):
                if not first:
                    sp.wait_ge(s_out[u], (n // SL) * 16)
                sp.dma_start(fx[:, u, :], x_v[n // B, n % B]).then_inc(s_xl[u], 16)
                sp.dma_start(fo[:, u, :], o_r[n // B, n % B]).then_inc(s_xl[u], 16)
                sp.dma_start(fog[:, u, :], og_d[n]).then_inc(s_xl[u], 16)
                if not (first and u < 3):
                    store(n - 3, (u - 3) % SL)

            per_tile(sp, fetch, SL)
            for n in range(NT - 3, NT):
                store(n, n % SL)
            for u in range(SL):
                sp.wait_ge(s_out[u], 16 * (NT // SL))

        @block.gpsimd
        def _(pool):
            pool.memset(w_up[:, :], 0.0).then_inc(s_pool0, 1)
            pool.memset(zero[:, :], 0.0).then_inc(s_pool0, 1)
            pool.memset(ident[:, :], 0.0).then_inc(s_id, 1)
            pool.memset(tri[:, :], 1.0).then_inc(s_id, 1)
            pool.memset(ones[:, :], 1.0).then_inc(s_id, 1)
            pool.memset(neghalf[:, :], -0.5).then_inc(s_id, 1)
            pool.memset(inv_d[:, 0:1], 1.0 / D).then_inc(s_id, 1)
            pool.memset(inv_d[:, 1:2], EPS).then_inc(s_id, 1)
            for row, first, step in ((down8, E, -1), (thr, 0, MT), (tidx, 0, 1)):
                pool.iota(row[:, :], [[step, row.shape[1]]], base=first, channel_multiplier=0,
                          allow_small_or_imprecise_dtypes=True).then_inc(s_id, 1)
            pool.wait_ge(s_id, 9)
            pool.affine_select(out=ident[:, :], in_=ident[:, :], compare_op=ALU.not_equal, fill=1.0,
                               base=0, pattern=[[-1, P]], channel_multiplier=1).then_inc(s_id, 1)
            pool.affine_select(out=tri[:, :], in_=tri[:, :], compare_op=ALU.is_gt, fill=0.0,
                               base=0, pattern=[[1, P]], channel_multiplier=-1).then_inc(s_id, 1)
            for j in range(NTB):
                pool.wait_ge(s_var, j + 1)
                pool.tensor_tensor(rstd[:, j * B:(j + 1) * B], var[:, j * B:(j + 1) * B],
                                   neghalf[:, 0:B], ALU.pow).then_inc(s_rstd, 1)

            def factors(n, u, first, last):
                pool.wait_ge(s_gam, n + 1)
                pool.wait_ge(s_ssm, n + 1)
                if not first:
                    pool.wait_ge(s_rec, n - 1)
                pool.tensor_tensor(rinv[:, u, :], ssm[:, u, :], neghalf[:, 0:H], ALU.pow).then_inc(s_pA, 1)
                pool.tensor_scalar(ngam[:, u, :], gam[:, u, :], -1.0, None, ALU.mult).then_inc(s_pA, 1)
                pool.wait_ge(s_pA, n * 2 + 2)
                pool.tensor_tensor(ngam[:, u, :], ngam[:, u, :], rinv[:, u, :], ALU.mult).then_inc(s_ng, 1)

            per_tile(pool, factors)
            pool.wait_ge(s_zero, 16 * NT)
            pool.wait_ge(s_slot, 2)
            pool.wait_ge(s_xTc, NT)

            pool.tensor_copy(idx[:, :], slot[:, :, :].rearrange("p t c -> p (t c)")).then_inc(s_idx, 1)
            pool.wait_ge(s_idx, 1)
            for n in range(NT):
                for c in range(2):
                    pool.indirect_dma_start(xs_d, bass.IndirectOffsetOnAxis(idx[:, 2 * n + c:2 * n + c + 1], 0),
                                            x_acc[:, n, :], None).then_inc(s_sc, 16)
            pool.wait_ge(s_sc, 32 * NT)
            for u in range(2):
                pool.wait_ge(s_yd[u], 16 * ((NM + 1 - u) // 2))
            for n in range(NT):
                for c, rows in enumerate((x_acc[:, n, :], wts[:, n * D:(n + 1) * D])):
                    pool.indirect_dma_start(rows, None, y_d, bass.IndirectOffsetOnAxis(idx[:, 2 * n + c:2 * n + c + 1], 0))\
                        .then_inc(s_gat, 16)

            def gate(n, u):
                pool.wait_ge(s_sz, n + 1)
                pool.tensor_tensor(x_acc[:, n, :], zg[:, u, :], szg[:, u, :], ALU.mult).then_inc(s_g2, 1)

            def mix(n, u, first, last):
                pool.wait_ge(s_wy, n + 1)
                pool.tensor_tensor(ym[:, :], wy[:, 0, :], wy[:, 1, :], ALU.add).then_inc(s_ym, 1)
                pool.wait_ge(s_sq, n + 1)
                pool.wait_ge(s_sq, n + 1)
                pool.tensor_tensor(gst[:, 3:4], gst[:, 2:3], inv_d[:, 0:1], ALU.mult).then_inc(s_gP, 1)
                pool.wait_ge(s_gP, n * 3 + 1)
                pool.tensor_tensor(gst[:, 3:4], gst[:, 3:4], inv_d[:, 1:2], ALU.add).then_inc(s_gP, 1)
                pool.wait_ge(s_gP, n * 3 + 2)
                pool.tensor_tensor(gst[:, 4:5], gst[:, 3:4], neghalf[:, 0:1], ALU.pow).then_inc(s_yr, 1)
                if not (first and u == 0):
                    gate(n - 1, (u + 1) % 2)
                pool.wait_ge(s_yn, n + 1)
                pool.tensor_tensor(zg[:, u, :], yn[:, :], gam_bc[:, :], ALU.mult).then_inc(s_gP, 1)
                pool.wait_ge(s_gP, n * 3 + 3)
                pool.tensor_tensor(zg[:, u, :], zg[:, u, :], bet_bc[:, :], ALU.add).then_inc(s_z, 1)

            pool.wait_ge(s_c, 16 * N_C)
            per_tile(pool, mix)
            gate(NT - 1, 1)

            def sum_up(n, u):
                pool.wait_ge(s_sgm, n + 1)
                pool.tensor_tensor(fx[:, u, :], fx[:, u, :], f_sg[:, u, :], ALU.add).then_inc(s_res, 1)

            def finish(n, u, first, last):
                pool.wait_ge(s_v1, n + 1)
                pool.tensor_tensor(crs[:, u:u + 1], cve[:, u:u + 1], neghalf[:, 0:1], ALU.pow).then_inc(s_r1, 1)
                if not (first and u < 2):
                    sum_up(n - 2, (u - 2) % SL)

            per_tile(pool, finish, SL)
            for n in (NT - 2, NT - 1):
                sum_up(n, n % SL)

        @block.scalar
        def _(act):
            def turned(n, u, first):
                act.wait_ge(s_T, n + 1)
                if not first:
                    act.wait_ge(s_L, n - 1)
                    act.wait_ge(s_Bp, n - 1)
                act.activation(xTs[u][:, :, :], psT[u][:, 0:D].rearrange("p (c t) -> p c t", c=KC), ACT.Copy)\
                    .then_inc(s_xTs, 1)

            def silus(n, u4, first, last):
                u = u4 % 2
                first, last, no_record = first and u4 < 2, last and u4 >= RS - 2, first
                act.wait_ge(s_xn, n + 1)
                act.activation(x_acc[:, n, :], xn[:, u, :], ACT.Copy).then_inc(s_xTc, 1)
                act.wait_ge(s_L, n + 1)
                if not first:
                    act.wait_ge(s_Fp, n - 1)
                act.activation(t1[u][:, :], psT[u][0:2 * HD, D:D + P], ACT.Copy).then_inc(s_t1, 1)
                if not (last and u == 1):
                    turned(n + 1, (u + 1) % 2, first and u == 0)
                act.wait_ge(s_A, n + 1)
                if not first:
                    act.wait_ge(s_kq, n * 2 - 2)
                act.activation(sg[:, u, :], psA[u][:, :], ACT.Sigmoid).then_inc(s_sg, 1)
                act.wait_ge(s_Bp, n + 1)
                if not first:
                    act.wait_ge(s_rec, n - 1)
                    act.wait_ge(s_ogd[u], (n // 2) * 16)
                if not no_record:
                    act.wait_ge(s_recd[u4], (n // RS) * 16)
                act.activation(gam[:, u, :], psB[u][:, D:D + H], ACT.Sigmoid).then_inc(s_gam, 1)
                act.activation(rec[:, u4, :, V_:V_ + HD], psB[u][:, 0:D].rearrange("p (h c) -> p h c", h=H), ACT.Copy)\
                    .then_inc(s_v, 1)
                act.wait_ge(s_Fp, n + 1)
                act.activation(rec[:, u4, :, F_:F_ + HD], psF[u][:, 0:D].rearrange("p (h c) -> p h c", h=H), ACT.Sigmoid)\
                    .then_inc(s_f, 1)
                act.activation(ogs[:, u, :], psF[u][:, D:2 * D], ACT.Sigmoid).then_inc(s_og, 1)
                act.wait_ge(s_f, n + 1)
                act.activation(f2[:, u, :].rearrange("p (h c) -> p h c", h=H), rec[:, u4, :, F_:F_ + HD], ACT.Square)\
                    .then_inc(s_f2, 1)

            turned(0, 0, True)
            per_tile(act, silus, RS)
            act.wait_ge(s_gt, 1)
            act.activation(gw[:, 0, :, :], gw[:, 0, :, :], ACT.Exp).then_inc(s_exp, 1)
            act.wait_ge(s_b1t, 1)
            act.activation(b1_sb[:, :], psT[0][:, 0:E * FC], ACT.Copy).then_inc(s_b1, 1)
            act.wait_ge(s_c, 16 * N_C)
            act.activation(wo_sb[:, 0, :], wo_sb[:, 0, :], ACT.Copy, scale=nw[:, 0:1]).then_inc(s_hb, 4)
            act.activation(wo_sb[:, 1, :], wo_sb[:, 1, :], ACT.Copy, scale=nw[:, 1:2]).then_inc(s_ys, 2)
            act.wait_ge(s_b1, 1)
            act.wait_ge(s_slot, 2)
            act.wait_ge(s_rec, NT)
            act.wait_ge(s_kq, 2 * NT)
            for u in range(RS):
                act.wait_ge(s_recd[u], 16 * (NT // RS))
            for u in range(2):
                act.wait_ge(s_ogd[u], 16 * (NT // 2))

            def expert_of(t):
                return act.value_load(etab[0:1, bass.ds(t, 1)], min_val=0, max_val=E - 1)

            def load_w1(e, v):
                act.dma_start(w1_sb[v][:, :, :], w1_v[e]).then_inc(s_w1d[v], 16)

            def load_w2(e, v):
                act.dma_start(w2_sb[v][:, :, :], w2_v[e]).then_inc(s_w2d[v], 16)

            def load_rows(t, v):
                act.dma_start(xg[v][:, :, :], xs_v[t]).then_inc(s_xg[v], 16)

            def turn_rows(t, v):
                act.wait_ge(s_xgT, t + 1)
                act.activation(xgT[:, :, :], psT[v][:, :].rearrange("p (c t) -> p c t", c=KC), ACT.Copy).then_inc(s_xgs, 1)

            def expert_tile(t, v, first, last):
                e = act.value_load(etab[0:1, bass.ds(t, 1)], min_val=0, max_val=E - 1)
                for m in range(FC):
                    act.wait_ge(s_h, t * FC + (m + 1))
                    act.activation(hT[:, m, :], ph[m % 4][:, 0:MT], ACT.Gelu,
                                   bias=b1_sb[:, bass.ds(e * FC + m, 1)]).then_inc(s_hb, 1)
                if last == 0:
                    later = expert_of(t + 2)
                    load_rows(t + 2, v)
                    load_w1(later, v)
                if last < 2:
                    turn_rows(t + 1, 1 - v)
                for q in range(MH):
                    act.wait_ge(s_y, t * MH + (q + 1))
                    if not first:
                        act.wait_ge(s_yd[v], (t // 2) * 16)
                    act.activation(ysb[v][:, q, :], psF[q][:, 0:D], ACT.Copy).then_inc(s_ys, 1)
                if last == 0:
                    load_w2(later, v)
                act.wait_ge(s_ys, t * MH + (MH + 2))
                act.dma_start(y_v[t], ysb[v][:, :, :]).then_inc(s_yd[v], 16)

            for t in range(2):
                e = expert_of(t)
                load_w1(e, t)
                load_w2(e, t)
            act.wait_ge(s_sc, 32 * NT)
            for t in range(2):
                load_rows(t, t)
            turn_rows(0, 0)
            for t in range(2):
                expert_tile(t, t, True, 0)
            with act.Fori(1, (NM - 3) // 2) as tp:
                for v in range(2):
                    expert_tile(tp * 2 + v, v, False, 0)
            for t in range(NM - 3, NM):
                expert_tile(t, t % 2, False, max(0, t - (NM - 3)))

            def norm(n, u, first, last):
                if not (first and u == 0):
                    act.wait_ge(s_ym, n)
                for c, rows in enumerate((x_acc[:, n, :], wts[:, bass.ds(n * D, D)])):
                    act.activation(wy[:, c, :], rows, ACT.Copy, scale=gs_flat[:, bass.ds(n + (2 + 2 * c) * NT, 1)])\
                        .then_inc(s_wy if c else s_wy0, 1)
                act.wait_ge(s_ym, n + 1)
                act.activation(yn[:, :], ym[:, :], ACT.Copy, accum_out=gst[:, 0:1]).then_inc(s_gA, 1)
                act.wait_ge(s_gA, n * 3 + 1)
                act.activation(gst[:, 1:2], gst[:, 0:1], ACT.Copy, scale=-1.0 / D).then_inc(s_gA, 1)
                act.wait_ge(s_gA, n * 3 + 2)
                act.activation(ym[:, :], ym[:, :], ACT.Identity, bias=gst[:, 1:2]).then_inc(s_gA, 1)
                act.wait_ge(s_gA, n * 3 + 3)
                act.activation(yn[:, :], ym[:, :], ACT.Square, accum_out=gst[:, 2:3]).then_inc(s_sq, 1)
                act.wait_ge(s_sq, n + 1)
                act.wait_ge(s_yr, n + 1)
                act.activation(yn[:, :], ym[:, :], ACT.Copy, scale=gst[:, 4:5]).then_inc(s_yn, 1)
                act.wait_ge(s_z, n + 1)
                act.activation(szg[:, u, :], zg[:, u, :], ACT.Sigmoid).then_inc(s_sz, 1)

            act.wait_ge(s_gat, 32 * NT)
            per_tile(act, norm)

            def turn_o(n, u, v, first):
                act.wait_ge(s_oT, n + 1)
                if not first:
                    act.wait_ge(s_s, n - 1)
                act.activation(oTs[v][:, :, :], psT[v][:, 0:D].rearrange("p (c t) -> p c t", c=KC), ACT.Copy)\
                    .then_inc(s_oTs, 1)

            def turn_tile(n, u, first, last):
                turn_o(n, u, u % 2, first and u < 2)

            per_tile(act, turn_tile, SL)

        @block.tensor
        def _(pe):
            def turn(n, u, first):
                pe.wait_ge(s_xn, n + 1)
                if not first:
                    pe.wait_ge(s_t1, n - 1)
                for c in range(KC):
                    mm = pe.transpose(psT[u][:, c * P:(c + 1) * P], xn[:, u, c * P:(c + 1) * P], ident[:, :])
                mm.then_inc(s_T, 1)

            def project(n, u, first, last):
                if not (last and u == 1):
                    turn(n + 1, (u + 1) % 2, first and u == 0)
                pe.wait_ge(s_xTs, n + 1)
                for c in range(KC):
                    mm = pe.matmul(psT[u][0:2 * HD, D:D + P], w_low[:, c, :], xTs[u][:, c, :],
                                   start=(c == 0), stop=(c == KC - 1))
                mm.then_inc(s_L, 1)
                if not first:
                    pe.wait_ge(s_kq, n * 2 - 2)
                for c in range(KC):
                    mm = pe.matmul(psA[u][:, :], xTs[u][:, c, :], w_kq[:, c, :], start=(c == 0), stop=(c == KC - 1))
                mm.then_inc(s_A, 1)
                if not first:
                    pe.wait_ge(s_v, n - 1)
                    pe.wait_ge(s_lg, n - 1)
                for c in range(KC):
                    mm = pe.matmul(psB[u][:, 0:D + H + E], xTs[u][:, c, :], w_vgg[:, c, :],
                                   start=(c == 0), stop=(c == KC - 1))
                mm.then_inc(s_Bp, 1)
                pe.wait_ge(s_t1, n + 1)
                if not first:
                    pe.wait_ge(s_og, n - 1)
                pe.matmul(psF[u][:, :], t1[u][:, :], w_up[:, :], start=True, stop=True).then_inc(s_Fp, 1)

            pe.wait_ge(s_id, 11)
            turn(0, 0, True)
            pe.wait_ge(s_w, 16 * N_W)
            per_tile(pe, project)
            pe.wait_ge(s_c, 16 * N_C)
            pe.transpose(psT[0][:, 0:E * FC], b1_rows[:, :], ident[0:E * FC, 0:E * FC]).then_inc(s_b1t, 1)
            pe.wait_ge(s_kq, 2 * NT)
            pe.wait_ge(s_lg, NT)
            pe.wait_ge(s_sel, 1)
            pe.wait_ge(s_b1, 1)
            pe.matmul(psT[0][:, 0:NT * E], tri[:, :], sel, start=True, stop=True).then_inc(s_cnt, 1)
            pe.matmul(psT[1][:, 0:NT * E], ones[:, :], sel, start=True, stop=True).then_inc(s_cnt, 1)
            pe.wait_ge(s_slot, 2)

            def turn_rows(t, v, nth):
                pe.wait_ge(s_xg[v], nth * 16 + 16)
                for c in range(KC):
                    for q in range(MH):
                        mm = pe.transpose(psT[v][:, c * MT + q * P:c * MT + (q + 1) * P],
                                          xg[v][:, q, c * P:(c + 1) * P], ident[:, :])
                mm.then_inc(s_xgT, 1)

            def expert_tile(t, v, nth, last):
                pe.wait_ge(s_w1d[v], nth * 16 + 16)
                pe.wait_ge(s_w2d[v], nth * 16 + 16)
                pe.wait_ge(s_xgs, t + 1)
                for m in range(FC):
                    pe.wait_ge(s_hb, t * FC + (m + 1))
                    for c in range(KC):
                        mm = pe.matmul(ph[m % 4][:, 0:MT], w1_sb[v][:, c, m * P:(m + 1) * P], xgT[:, c, :],
                                       start=(c == 0), stop=(c == KC - 1))
                    mm.then_inc(s_h, 1)
                if not last:
                    turn_rows(t + 1, 1 - v, nth + v)
                e = pe.value_load(etab[0:1, bass.ds(t, 1)], min_val=0, max_val=E - 1)
                for q in range(MH):
                    pe.wait_ge(s_ys, t * MH + (q + 1))
                    for m in range(FC):
                        if q == 0:
                            pe.wait_ge(s_hb, t * FC + (m + 5))
                        pe.matmul(psF[q][:, 0:D], hT[:, m, q * P:(q + 1) * P], w2_sb[v][:, m, :],
                                  start=(m == 0), stop=False)
                    pe.matmul(psF[q][:, 0:D], ones[0:1, :], b2_flat[:, bass.ds(e * D, D)], start=False, stop=True)\
                        .then_inc(s_y, 1)

            turn_rows(0, 0, 0)
            with pe.Fori(0, (NM - 1) // 2) as tp:
                for v in range(2):
                    expert_tile(tp * 2 + v, v, tp, False)
            expert_tile(NM - 1, 0, (NM - 1) // 2, True)

            def turn_o(n, u, first):
                v = u % 2
                pe.wait_ge(s_on, n + 1)
                if not first:
                    pe.wait_ge(s_oTs, n - 1)
                for c in range(KC):
                    mm = pe.transpose(psT[v][:, c * P:(c + 1) * P], f_on[:, u, c * P:(c + 1) * P], ident[:, :])
                mm.then_inc(s_oT, 1)

            def out_product(n, u, first, last):
                turn_o(n, u, first and u < 2)
                pe.wait_ge(s_oTs, n + 1)
                if not (first and u < 2):
                    pe.wait_ge(s_sgm, n - 1)
                for c in range(KC):
                    mm = pe.matmul(psA[u % 2][:, 0:D], oTs[u % 2][:, c, :], wo_sb[:, c, :],
                                   start=(c == 0), stop=(c == KC - 1))
                mm.then_inc(s_s, 1)

            per_tile(pe, out_product, SL)

        @block.vector
        def _(dve):
            for j in range(NTB):
                dve.wait_ge(s_x[j], 16 * B)
                with dve.Fori(0, B) as b_:
                    dve.bn_stats(stats_flat[:, bass.ds((b_ + j * B) * 6, 6)], x_acc[:, b_ + j * B, :]).then_inc(s_st, 1)
                dve.wait_ge(s_st, B * (j + 1))
                st = stats[:, j * B:(j + 1) * B, :]
                me, mo, ve, vo = st[:, :, 1], st[:, :, 4], st[:, :, 2], st[:, :, 5]
                dve.tensor_tensor(lt[:, 0, :], me, mo, ALU.add).then_inc(s_stc, 1)
                dve.tensor_tensor(lt[:, 1, :], me, mo, ALU.subtract).then_inc(s_stc, 1)
                dve.tensor_tensor(lt[:, 2, :], ve, vo, ALU.add).then_inc(s_stc, 1)
                dve.wait_ge(s_stc, 5 * j + 2)
                dve.tensor_scalar(mean[:, j * B:(j + 1) * B], lt[:, 0, :], 0.5, None, ALU.mult).then_inc(s_stc, 1)
                dve.scalar_tensor_tensor(out=lt[:, 3, :], in0=lt[:, 1, :], scalar=D / 4.0, in1=lt[:, 1, :],
                                         op0=ALU.mult, op1=ALU.mult).then_inc(s_stc, 1)
                dve.wait_ge(s_stc, 5 * j + 5)
                dve.tensor_tensor(lt[:, 3, :], lt[:, 3, :], lt[:, 2, :], ALU.add).then_inc(s_lt, 1)
                dve.wait_ge(s_lt, j + 1)
                dve.tensor_scalar(var[:, j * B:(j + 1) * B], lt[:, 3, :], 1.0 / D, EPS, ALU.mult, ALU.add).then_inc(s_var, 1)

            def normalise(n, u, first):
                if not first:
                    dve.wait_ge(s_T, n - 1)
                    dve.wait_ge(s_xTc, n - 1)
                dve.tensor_scalar(xn[:, u, :], x_acc[:, n, :], mean[:, bass.ds(n, 1)], rstd[:, bass.ds(n, 1)],
                                  ALU.subtract, ALU.mult).then_inc(s_xn, 1)

            def heads(row):
                return row.rearrange("p (h c) -> p h c", h=H)

            def factors(n, u, u4, first):
                dve.wait_ge(s_pA, n * 2 + 2)
                dve.tensor_tensor(rec[:, u4, :, K_:K_ + HD], heads(kraw[:, u, :]),
                                  rinv[:, u, :].unsqueeze(2).broadcast_to([P, H, HD]), ALU.mult).then_inc(s_kg, 1)
                dve.wait_ge(s_ng, n + 1)
                if not first:
                    dve.wait_ge(s_rec, n)
                dve.tensor_tensor(heads(kgam[:, :]), heads(kraw[:, u, :]),
                                  ngam[:, u, :].unsqueeze(2).broadcast_to([P, H, HD]), ALU.mult).then_inc(s_kg, 1)
                dve.wait_ge(s_kg, n * 2 + 2)
                dve.wait_ge(s_f2, n + 1)
                dve.tensor_tensor(rec[:, u4, :, A_:A_ + HD], heads(kgam[:, :]), heads(f2[:, u, :]), ALU.mult).then_inc(s_rec, 1)

            def silus(n, u4, first, last):
                u = u4 % 2
                dve.wait_ge(s_sg, n + 1)
                if not first:
                    dve.wait_ge(s_recd[u4], (n // RS) * 16)
                if not (first and u4 < 2):
                    dve.wait_ge(s_ng, n - 1)
                dve.tensor_tensor(kraw[:, u, :], psA[u][:, 0:D], sg[:, u, 0:D], ALU.mult).then_inc(s_kq, 1)
                dve.tensor_tensor(rec[:, u4, :, Q_:Q_ + HD], heads(psA[u][:, D:2 * D]), heads(sg[:, u, D:2 * D]), ALU.mult)\
                    .then_inc(s_kq, 1)
                dve.wait_ge(s_kq, n * 2 + 1)
                dve.tensor_tensor(ksq[:, :], kraw[:, u, :], kraw[:, u, :], ALU.mult).then_inc(s_ksq, 1)
                if not (last and u4 >= RS - 2):
                    normalise(n + 2, u, False)
                dve.wait_ge(s_ksq, n * 2 + 1)
                dve.tensor_reduce(ss[:, u, :], heads(ksq[:, :]), AX.X, ALU.add).then_inc(s_ksq, 1)
                dve.wait_ge(s_v, n + 1)
                dve.tensor_tensor(logits[:, n, :], psB[u][:, D + H:D + H + E], bg_bc[:, :], ALU.add).then_inc(s_lg, 1)
                dve.wait_ge(s_ksq, n * 2 + 2)
                dve.tensor_scalar(ssm[:, u, :], ss[:, u, :], 1e-24, None, ALU.max).then_inc(s_ssm, 1)
                if not (first and u4 == 0):
                    factors(n - 1, 1 - u, (u4 - 1) % RS, first and u4 == 1)

            dve.wait_ge(s_rstd, NTB)
            for n in range(2):
                normalise(n, n, True)
            dve.wait_ge(s_w, 16 * N_W)
            per_tile(dve, silus, RS)
            factors(NT - 1, 1, RS - 1, False)

            wide = [P, NT, E]

            def over_e(v):
                return gs[:, v, :].unsqueeze(2).broadcast_to(wide)

            rank = down8[:, :].unsqueeze(1).broadcast_to(wide)
            done = [0]

            def link(ins):
                ins.then_inc(s_dG, 1)
                done[0] += 1
                dve.wait_ge(s_dG, done[0])

            ex, pr, m1, rest_, m2 = (gw[:, i, :, :] for i in range(5))
            dve.wait_ge(s_lg, NT)
            dve.wait_ge(s_id, 11)
            link(dve.tensor_reduce(gs[:, 0, :], logits[:, :, :], AX.X, ALU.max))
            dve.tensor_tensor(ex, logits[:, :, :], over_e(0), ALU.subtract).then_inc(s_gt, 1)
            dve.wait_ge(s_exp, 1)
            link(dve.tensor_reduce(gs[:, 1, :], ex, AX.X, ALU.add))
            link(dve.reciprocal(gs[:, 1, :], gs[:, 1, :]))
            link(dve.tensor_tensor(pr, ex, over_e(1), ALU.mult))

            def largest(values, top, at, mask):
                link(dve.tensor_reduce(gs[:, top, :], values, AX.X, ALU.max))
                link(dve.tensor_tensor(mask, values, over_e(top), ALU.is_equal))
                link(dve.tensor_tensor(mask, mask, rank, ALU.mult))
                link(dve.tensor_reduce(gs[:, at, :], mask, AX.X, ALU.max))
                link(dve.tensor_tensor(mask, rank, over_e(at), ALU.is_equal))

            largest(pr, 2, 3, m1)
            link(dve.scalar_tensor_tensor(out=rest_.rearrange("p t e -> p (t e)"), in0=m1.rearrange("p t e -> p (t e)"),
                                          scalar=-2.0, in1=pr.rearrange("p t e -> p (t e)"), op0=ALU.mult, op1=ALU.add))
            largest(rest_, 4, 5, m2)
            dve.tensor_tensor(sel.rearrange("p (t e) -> p t e", e=E), m1, m2, ALU.add).then_inc(s_sel, 1)
            link(dve.tensor_tensor(gs[:, 0, :], gs[:, 2, :], gs[:, 4, :], ALU.add))
            link(dve.tensor_scalar(gs[:, 0, :], gs[:, 0, :], 1e-8, None, ALU.add))
            link(dve.reciprocal(gs[:, 0, :], gs[:, 0, :]))
            link(dve.tensor_tensor(gs[:, 2, :], gs[:, 2, :], gs[:, 0, :], ALU.mult))
            link(dve.tensor_tensor(gs[:, 4, :], gs[:, 4, :], gs[:, 0, :], ALU.mult))
            dve.wait_ge(s_cnt, 2)
            link(dve.tensor_copy(tot[:, :, :], psT[1][:, 0:NT * E].rearrange("p (t e) -> p t e", e=E)))
            for e in range(E):
                link(dve.tensor_tensor_scan(cum[:, :, e], ones[:, 0:NT], tot[:, :, e], 0.0, ALU.mult, ALU.add))
            link(dve.tensor_tensor(cmp16[:, :, :], cum[:, NT - 1, :].unsqueeze(2).broadcast_to([P, E, B * T // MT]),
                                   thr[:, :].unsqueeze(1).broadcast_to([P, E, B * T // MT]), ALU.is_gt))
            link(dve.tensor_reduce(nte[:, 0, :], cmp16[:, :, :], AX.X, ALU.add))
            link(dve.tensor_tensor_scan(nte[:, 1, :], ones[:, 0:E], nte[:, 0, :], 0.0, ALU.mult, ALU.add))
            link(dve.tensor_tensor(nte[:, 2, :], nte[:, 1, :], nte[:, 0, :], ALU.subtract))
            link(dve.tensor_scalar(nte[:, 2, :], nte[:, 2, :], float(MT), None, ALU.mult))
            link(dve.tensor_tensor(cum[:, :, :], cum[:, :, :], tot[:, :, :], ALU.subtract))
            link(dve.tensor_tensor(cum[:, :, :], cum[:, :, :], psT[0][:, 0:NT * E].rearrange("p (t e) -> p t e", e=E), ALU.add))
            link(dve.tensor_tensor(cum[:, :, :], cum[:, :, :], nte[:, 2, :].unsqueeze(1).broadcast_to(wide), ALU.add))
            for c, mask in enumerate((m1, m2)):
                link(dve.tensor_tensor(mask, mask, cum[:, :, :], ALU.mult))
                link(dve.tensor_reduce(slot[:, :, c], mask, AX.X, ALU.add))
            across = [P, NM, E - 1]
            link(dve.tensor_tensor(cmpt[:, :, :], tidx[:, :].unsqueeze(2).broadcast_to(across),
                                   nte[:, 1, 0:E - 1].unsqueeze(1).broadcast_to(across), ALU.is_ge))
            link(dve.tensor_reduce(etab_f[:, :], cmpt[:, :, :], AX.X, ALU.add))
            dve.tensor_copy(etab[:, :], etab_f[:, :]).then_inc(s_slot, 2)

            def state(s):
                return ring[:, s, S_OFF:S_OFF + HD * HD]

            def step(s, u, t):
                old, new = (state(x).rearrange("p (k v) -> p k v", k=HD) for x in ((s - 1) % RING, s))
                both = ring2[:, s, :, 0:HD * HD].rearrange("p two (k v) -> p two k v", k=HD)
                rows = ring[:, s, 0:S_OFF].rearrange("p (k v) -> p v k", v=HD)
                ku = qbuf[:, :].rearrange("p (k v) -> p k v", k=HD)
                cols = [slice(h * VH, (h + 1) * VH) for h in range(2)]
                for h, c in enumerate(cols):
                    dve.wait_ge(s_half[h], t * 4 + 1)
                    dve.tensor_tensor(
                        both[:, :, :, c], old[:, :, c].unsqueeze(1).broadcast_to([P, 2, HD, VH]),
                        rbh[:, u, s, A_:A_ + 2 * HD].rearrange("p (two k) -> p two k", two=2).unsqueeze(3)
                        .broadcast_to([P, 2, HD, VH]), ALU.mult).then_inc(s_half[h], 1)
                for h, c in enumerate(cols):
                    dve.wait_ge(s_half[h], t * 4 + 2)
                    dve.tensor_reduce(ubuf[:, c], rows[:, c, :], AX.X, ALU.add).then_inc(s_half[h], 1)
                for h, c in enumerate(cols):
                    dve.wait_ge(s_half[h], t * 4 + 3)
                    dve.tensor_tensor(ku[:, :, c], rbh[:, u, s, K_:K_ + HD].unsqueeze(2).broadcast_to([P, HD, VH]),
                                      ubuf[:, c].unsqueeze(1).broadcast_to([P, HD, VH]), ALU.mult).then_inc(s_half[h], 1)
                for h, c in enumerate(cols):
                    dve.wait_ge(s_half[h], t * 4 + 4)
                    dve.tensor_tensor(new[:, :, c], new[:, :, c], ku[:, :, c], ALU.add).then_inc(s_half[h], 1)

            def half(c, u, r):
                lo = r * HALF
                dve.tensor_copy(ring[:, lo:lo + HALF, HD * HD:S_OFF], rbh[:, u, lo:lo + HALF, V_:V_ + HD]).then_inc(s_vr, 1)
                dve.wait_ge(s_vr, c * 2 + (r + 1))
                for s in range(lo, lo + HALF):
                    step(s, u, c * RING + s)
                for h in range(2):
                    dve.wait_ge(s_half[h], c * (RING * 4) + ((lo + HALF) * 4 + 1))
                prod = ring[:, lo:lo + HALF, 0:HD * HD]
                dve.tensor_tensor(prod.rearrange("p s (k v) -> p s k v", k=HD),
                                  ring[:, lo:lo + HALF, S_OFF:S_OFF + HD * HD].rearrange("p s (k v) -> p s k v", k=HD),
                                  rbh[:, u, lo:lo + HALF, Q_:Q_ + HD].unsqueeze(3).broadcast_to([P, HALF, HD, HD]),
                                  ALU.mult).then_inc(s_om, 1)
                dve.wait_ge(s_om, c * 2 + (r + 1))
                dve.tensor_reduce(obh[:, u, lo:lo + HALF, :], prod.rearrange("p s (k v) -> p s v k", k=HD), AX.X, ALU.add)\
                    .then_inc(s_o, 1)

            def chunk(c, u, arrived, first):
                dve.wait_ge(s_rb[u], arrived)
                if not first:
                    dve.wait_ge(s_od[u], arrived - 16 * B)
                for r in range(2):
                    half(c, u, r)

            for h in range(2):
                dve.memset(state(RING - 1).rearrange("p (k v) -> p k v", k=HD)[:, :, h * VH:(h + 1) * VH], 0.0)\
                    .then_inc(s_half[h], 1)
            for c in range(2):
                chunk(c, c, 16 * B, True)
            with dve.Fori(1, NCH // 2) as cp:
                for u in range(2):
                    chunk(cp * 2 + u, u, cp * (16 * B) + 16 * B, False)

            for u in range(2):
                dve.wait_ge(s_yd[u], 16 * ((NM + 1 - u) // 2))

            def norms(n, u, nth):
                dve.wait_ge(s_xl[u], nth * 48 + 48)
                dve.tensor_tensor(f_on[:, u, :], fo[:, u, :], fog[:, u, :], ALU.mult).then_inc(s_dC, 1)
                dve.wait_ge(s_dC, n * 8 + 1)
                dve.bn_stats(cst[:, u, :], f_on[:, u, :]).then_inc(s_dC, 1)
                dve.wait_ge(s_dC, n * 8 + 2)
                me, mo, ve, vo = (cst[:, u, i:i + 1] for i in (1, 4, 2, 5))
                dve.tensor_tensor(cmv[:, u, 1:2], me, mo, ALU.subtract).then_inc(s_dC, 1)
                dve.tensor_tensor(cmv[:, u, 2:3], ve, vo, ALU.add).then_inc(s_dC, 1)
                dve.tensor_tensor(cmv[:, u, 0:1], me, mo, ALU.add).then_inc(s_dC, 1)
                dve.wait_ge(s_dC, n * 8 + 4)
                dve.scalar_tensor_tensor(out=cmv[:, u, 1:2], in0=cmv[:, u, 1:2], scalar=D / 4.0, in1=cmv[:, u, 1:2],
                                         op0=ALU.mult, op1=ALU.mult).then_inc(s_dC, 1)
                dve.wait_ge(s_dC, n * 8 + 5)
                dve.tensor_scalar(cmv[:, u, 0:1], cmv[:, u, 0:1], 0.5, None, ALU.mult).then_inc(s_dC, 1)
                dve.wait_ge(s_dC, n * 8 + 6)
                dve.tensor_tensor(cmv[:, u, 2:3], cmv[:, u, 2:3], cmv[:, u, 1:2], ALU.add).then_inc(s_dC, 1)
                dve.wait_ge(s_dC, n * 8 + 8)
                dve.tensor_scalar(cve[:, u:u + 1], cmv[:, u, 2:3], 1.0 / D, EPS, ALU.mult, ALU.add).then_inc(s_v1, 1)

            def scale(n, u):
                dve.wait_ge(s_r1, n + 1)
                dve.tensor_scalar(f_on[:, u, :], f_on[:, u, :], cmv[:, u, 0:1], crs[:, u:u + 1],
                                  ALU.subtract, ALU.mult).then_inc(s_on, 1)

            def gated(n, u):
                dve.wait_ge(s_s, n + 1)
                dve.wait_ge(s_g2, NT)
                dve.tensor_tensor(f_sg[:, u, :], psA[u % 2][:, 0:D], x_acc[:, n, :], ALU.mult).then_inc(s_sgm, 1)

            def finish(n, u, first, last):
                if not (last and u == SL - 1):
                    norms(n + 1, (u + 1) % SL, (n + 1) // SL)
                scale(n, u)
                if not (first and u == 0):
                    gated(n - 1, (u - 1) % SL)

            norms(0, 0, 0)
            per_tile(dve, finish, SL)
            gated(NT - 1, (NT - 1) % SL)


_INS = ['L0_attn_x', 'L0_attn_Wq', 'L0_attn_Wk', 'L0_attn_Wv', 'L0_attn_Wgamma', 'L0_attn_Wf1', 'L0_attn_Wf2',
        'L0_attn_Wog1', 'L0_attn_Wog2', 'L0_attn_norm_w', 'L0_attn_Wo', 'L0_ffn_Wg', 'L0_ffn_bg', 'L0_ffn_W1',
        'L0_ffn_b1', 'L0_ffn_W2', 'L0_ffn_b2', 'L0_ffn_gamma', 'L0_ffn_beta']
_OUTS = [((B, T, D), 'float32')]


def kernel(**inputs):
    import numpy as _np
    import concourse.bacc as _bacc
    from concourse import mybir as _mybir
    from concourse.bass_utils import run_bass_kernel_spmd as _run

    nc = _bacc.Bacc("TRN2", target_bir_lowering=False, num_devices=1)
    arrays, args = {}, []
    for name in _INS:
        a = _np.ascontiguousarray(inputs[name])
        arrays[f"in_{name}_dram"] = a
        args.append(nc.dram_tensor(f"in_{name}_dram", a.shape, _mybir.dt.from_np(a.dtype), kind="ExternalInput").ap())
    for i, (shape, dtype) in enumerate(_OUTS):
        dt = _mybir.dt.from_np(_np.dtype(dtype))
        args.append(nc.dram_tensor(f"out_{i}_dram", shape, dt, kind="ExternalOutput").ap())
    build(nc, *args)
    r = _run(nc, [arrays], core_ids=[0])
    got = tuple(r.results[0][f"out_{i}_dram"] for i in range(len(_OUTS)))
    return got[0]
```
